# Optimizing a Trainium2 kernel written in Bass

```python
import numpy as np
import jax
import jax.numpy as jnp

def _softmax(x, axis=-1):
    return jax.nn.softmax(x, axis=axis)

def _gelu(x):
    return jax.nn.gelu(x, approximate=True)

def _silu(x):
    return jax.nn.silu(x)

def _sigmoid(x):
    return jax.nn.sigmoid(x)

def _layernorm(x, axis=-1, eps=1e-05):
    m = jnp.mean(x, axis=axis, keepdims=True)
    v = jnp.var(x, axis=axis, keepdims=True)
    return (x - m) / jnp.sqrt(v + eps)

def _scatter_add(tgt, idx, src, axis=0):
    return tgt.at[idx].add(src)

def _segment_sum(src, seg, n):
    return jax.ops.segment_sum(src, seg, n)
kernel_name = 'mk_adj_preln_d1_adj_r2_5d7581'

def setup_inputs(seed: int=0):
    np.random.seed(seed)
    _w = jnp.asarray

    def _rec_inputs():
        import jax
        import jax.numpy as jnp
        _gk = jax.random.key(seed)
        x = 7.22e-05 + 1 * jax.random.normal(jax.random.fold_in(_gk, 1), (64, 128, 512), jnp.float32)
        _a = jax.random.bernoulli(jax.random.fold_in(_gk, 2), 0.03125, (128, 128))
        _a = jnp.logical_or(_a, jnp.swapaxes(_a, -1, -2))
        _a = jnp.logical_or(_a, jnp.eye(128, dtype=bool))
        _af = _a.astype(jnp.float32)
        _af = _af * jax.random.uniform(jax.random.fold_in(_gk, 3), (128, 128), jnp.float32, 0.05, 0.108252)
        adj = _af
        return (x, adj)
    x, adj = _rec_inputs()

    def _L0_gnn_setup():
        import jax, jax.numpy as jnp
        import numpy as np

        def _ada_gcn(xn, weight, bias):
            N, B, L = xn.shape
            x_norm = xn / jnp.maximum(jnp.linalg.norm(xn, axis=-1, keepdims=True), 1e-12)
            mean_sim = jnp.einsum('nbl,mbl->nm', x_norm, x_norm) / B
            k = max(int(N * 0.3), 1)
            _, idx = jax.lax.top_k(mean_sim, k + 1)
            rows = jnp.arange(N)[:, None]
            non_self = idx != rows
            order = jnp.cumsum(non_self.astype(jnp.int32), axis=1) - 1
            keep = non_self & (order < k)
            mask = jnp.zeros((N, N), dtype=bool).at[jnp.broadcast_to(rows, idx.shape), idx].set(keep)
            A = jnp.where(mask, mean_sim, jnp.zeros((), mean_sim.dtype))
            deg = A.sum(axis=0)
            dinv = jnp.where(deg > 0, jax.lax.rsqrt(deg), jnp.zeros((), deg.dtype))
            An = dinv[:, None] * A * dinv[None, :]
            xw = jnp.einsum('nbl,lo->nbo', xn, weight)
            out = jnp.einsum('sd,sbl->dbl', An, xw) + bias
            return out
        key = jax.random.key(seed)
        k1, k2 = jax.random.split(key)
        B, L, N = (32, 128, 512)
        x = jax.random.normal(k1, (B, L, N), dtype=jnp.float32)
        limit = float(np.sqrt(6.0 / (L + L)))
        weight = jax.random.uniform(k2, (L, L), dtype=jnp.float32, minval=-limit, maxval=limit)
        bias = jnp.zeros((L,), dtype=jnp.float32)
        return {'x': x, 'weight': weight, 'bias': bias}
    _L0_gnn_all = _L0_gnn_setup()
    _L0_gnn_in = {k: v for k, v in _L0_gnn_all.items() if k in ('bias',)}
    del _L0_gnn_all
    return {'x': x, 'adj': adj, 'L0_gnn_bias': _L0_gnn_in['bias']}

def reference(x, adj, L0_gnn_bias):
    import jax
    import jax.numpy as jnp

    def _L0_gnn_ref(x, weight, bias):
        import jax, jax.numpy as jnp
        import numpy as np

        def _ada_gcn(xn, weight, bias):
            N, B, L = xn.shape
            x_norm = xn / jnp.maximum(jnp.linalg.norm(xn, axis=-1, keepdims=True), 1e-12)
            mean_sim = jnp.einsum('nbl,mbl->nm', x_norm, x_norm) / B
            k = max(int(N * 0.3), 1)
            _, idx = jax.lax.top_k(mean_sim, k + 1)
            rows = jnp.arange(N)[:, None]
            non_self = idx != rows
            order = jnp.cumsum(non_self.astype(jnp.int32), axis=1) - 1
            keep = non_self & (order < k)
            mask = jnp.zeros((N, N), dtype=bool).at[jnp.broadcast_to(rows, idx.shape), idx].set(keep)
            A = jnp.where(mask, mean_sim, jnp.zeros((), mean_sim.dtype))
            deg = A.sum(axis=0)
            dinv = jnp.where(deg > 0, jax.lax.rsqrt(deg), jnp.zeros((), deg.dtype))
            An = dinv[:, None] * A * dinv[None, :]
            xw = jnp.einsum('nbl,lo->nbo', xn, weight)
            out = jnp.einsum('sd,sbl->dbl', An, xw) + bias
            return out
        xn = jnp.transpose(x, (2, 0, 1))
        num_levels = 1
        for _ in range(num_levels):
            xn = _ada_gcn(xn, weight, bias)
        return jnp.transpose(xn, (1, 2, 0))
    h = jnp.maximum(_layernorm(x, axis=-1), 0.0)
    x = x + _L0_gnn_ref(h, adj, L0_gnn_bias)
    return x

_drawn_inputs = setup_inputs


def setup_inputs(seed=0):
    import zlib

    import numpy as np

    out = dict(_drawn_inputs(seed))
    spreads = {'L0_gnn_bias': (0.0, 0.1)}
    factors = {}
    for name, (base, spread) in spreads.items():
        noise = np.random.default_rng([zlib.crc32(name.encode()), seed]).standard_normal(out[name].shape)
        drawn = base * np.exp(spread * noise) if base else spread * noise
        out[name] = jnp.asarray(drawn.astype(out[name].dtype))
    for name, factor in factors.items():
        out[name] = (out[name] * factor).astype(out[name].dtype)
    return out
```

```python
import math

import concourse.bass as bass
from concourse import mybir
from contextlib import ExitStack


def normal_quantile(share):
    low, high = -8.0, 8.0
    for _ in range(60):
        z = (low + high) / 2
        if (1.0 + math.erf(z / math.sqrt(2.0))) / 2 < share:
            low = z
        else:
            high = z
    return (low + high) / 2


def adaptive_gcn_block(nc: bass.Bass, x: bass.AP, adj: bass.AP, bias: bass.AP, out: bass.AP):
    f32, f16, bf16, i32 = mybir.dt.float32, mybir.dt.float16, mybir.dt.bfloat16, mybir.dt.int32
    ALU = mybir.AluOpType
    ACT = mybir.ActivationFunctionType
    AX_X = mybir.AxisListType.X

    B, L, N = x.shape
    P = 128
    NC = N // P
    G = 2
    NS = 4
    NG = B // G
    LEAD = 3
    NQ = G * NC + G
    TOP = max(int(N * 0.3), 1)
    EPS = 1e-5
    XN_SCALE = 2.0 ** 14
    SIM_SCALE = 1.0 / (XN_SCALE * XN_SCALE * B)
    W_SCALE = 2.0 ** 13
    XW_SCALE = 2.0 ** 3
    NORM_SCALE = XW_SCALE / (XN_SCALE * W_SCALE)
    DINV_SCALE = 2.0 ** 6
    TOP_BIT = 29
    PICK = 16
    GOAL = TOP - PICK // 2
    QUANTILE = normal_quantile(1.0 - GOAL / (N - 1))
    DENSITY = N * math.exp(-QUANTILE * QUANTILE / 2) / math.sqrt(2 * math.pi)
    GAINS = (0.9, 0.7)
    SEGS = 4
    EARLY = 20
    EARLY_FLAG, EARLY_DEG, EARLY_ROW = 15, 17, 18
    EARLY_KEPT = 13
    EARLY_STD = 2
    EARLY_AN = 18
    MIX_BANKS = 4
    MADE = (EARLY, EARLY, EARLY + 1, EARLY + 2, EARLY + MIX_BANKS)

    x_v = x.rearrange("(g j) l n -> g l j n", j=G)
    out_v = out.rearrange("(g j) l n -> g l j n", j=G)

    ctx = ExitStack()
    with ctx:
        def sb(name, shape, dt=f32):
            return ctx.enter_context(nc.sbuf_tensor(name, shape, dt))

        def pb(name):
            return ctx.enter_context(nc.psum_tensor(name, [P, N], f32))

        def sem(name):
            return ctx.enter_context(nc.semaphore(name))

        parts = sb("parts", [P, B, 2, N], f16)
        x_ring = sb("x_ring", [P, NS, G, N])
        h_ring = sb("h_ring", [P, NS, G, N])
        squares = sb("squares", [P, 4, N])
        squares_lo = sb("squares_lo", [P, 4, N], f16)
        wide = sb("wide", [P, 4, N])
        sim = sb("sim", [P, NC, N])
        an_hi = sb("an_hi", [P, NC, N], f16)
        an_lo = sb("an_lo", [P, NC, N], f16)
        ident = sb("ident", [P, P])
        ones = sb("ones", [P, 1])
        ones_hi = sb("ones_hi", [P, 1], bf16)
        ones_lo = sb("ones_lo", [P, 1], f16)
        zeros = sb("zeros", [P, N], f16)
        node_norm = sb("node_norm", [P, B, NC])
        stats = sb("stats", [P, 2, G, 6])
        mean_var = sb("mean_var", [P, 4, G, 2])
        power = sb("power", [P, 4, NQ])
        root = sb("root", [P, 2, NQ])
        inv = sb("inv", [P, 4, NQ])
        inv_t = sb("inv_t", [P, 3, NQ])
        shift = sb("shift", [P, 4, G])
        w = sb("w", [P, P])
        w_hi = sb("w_hi", [P, P], f16)
        w_lo = sb("w_lo", [P, P], f16)
        w_t = sb("w_t", [P, 4])
        w_top = sb("w_top", [P, 1])
        bias_t = sb("bias_t", [P, 1])
        row_stats = sb("row_stats", [P, NC, 6])
        row_mean = sb("row_mean", [P, NC, 2])
        row_std = sb("row_std", [P, NC])
        per_count = sb("per_count", [P, NC])
        theta = sb("theta", [P, NC])
        move = sb("move", [P, NC])
        count = sb("count", [P, NC])
        order = sb("order", [P, PICK])
        rank_wanted = sb("rank_wanted", [P, NC])
        piece_largest = sb("piece_largest", [P, NC, SEGS, 8])
        piece_least = sb("piece_least", [P, NC])
        missed = sb("missed", [P, NC])
        largest = sb("largest", [P, NC, PICK])
        one_hot = sb("one_hot", [P, NC, PICK - 1])
        picked = sb("picked", [P, 2, NC, PICK - 1])
        value = sb("value", [P, 2, NC])
        unsure = sb("unsure", [P, 2, NC])
        unsure_any = sb("unsure_any", [P, 2])
        unsure_rows = sb("unsure_rows", [1, 2], i32)
        bit = sb("bit", [P, NC], i32)
        best = sb("best", [P, NC], i32)
        cand = sb("cand", [P, NC], i32)
        keep_bit = sb("keep_bit", [P, NC], i32)
        need = sb("need", [P, NC])
        above, equal, rank = squares[:, 0:1], squares[:, 1:2], squares[:, 2:3]
        diag_half = squares[:, 3].rearrange("p (c n) -> p c n", c=NC)
        adjacency = h_ring[:, 0:2].rearrange("p s g n -> p (s g) n")
        under = h_ring[:, 2:4].rearrange("p s g n -> p (s g) n")
        adjacency_lo = squares_lo
        deg = sb("deg", [P, NC])
        deg_root = sb("deg_root", [P, NC])
        deg_t = sb("deg_t", [P, 5, NC])
        dinv = sb("dinv", [P, NC])
        dinv_scaled = sb("dinv_scaled", [P, NC])
        d_top = sb("d_top", [P, 4])
        an_scale = sb("an_scale", [P, 1])
        out_scale = sb("out_scale", [P, 1])

        gram = [pb(f"gram{i}") for i in range(NC)]
        cross = pb("cross")
        small = pb("small")
        bank = [pb("bank0"), pb("bank1")]

        s_const = sem("s_const")
        s_memset = sem("s_memset")
        s_w_in = sem("s_w_in")
        x_first = [sem(f"x_first{j}") for j in range(G)]
        x_loaded = [sem(f"x_loaded{i}") for i in range(NS)]
        stats_ready = sem("stats_ready")
        mean_ready = sem("mean_ready")
        power_ready = sem("power_ready")
        root_ready = sem("root_ready")
        newton_a, newton_b, newton_c = sem("newton_a"), sem("newton_b"), sem("newton_c")
        inv_ready = sem("inv_ready")
        ln_ready = sem("ln_ready")
        norm_kept = sem("norm_kept")
        h_ready = sem("h_ready")
        square_ready = sem("square_ready")
        square_split = [sem("square_split_pool"), sem("square_split_dve")]
        summed = sem("summed")
        bcast_ready = sem("bcast_ready")
        wide_ready = sem("wide_ready")
        hi_ready = sem("hi_ready")
        lo_ready = sem("lo_ready")
        dve_step = sem("dve_step")
        norm_scaled = sem("norm_scaled")
        gram_done = sem("gram_done")
        w_max_ready = sem("w_max_ready")
        w_row_ready = sem("w_row_ready")
        w_split_ready = sem("w_split_ready")
        act_evac = sem("act_evac")
        dve_evac = sem("dve_evac")
        turned = sem("turned")
        diagonal_full = sem("diagonal_full")
        diagonal_read = sem("diagonal_read")
        lower_full = sem("lower_full")
        sim_ready = sem("sim_ready")
        row_std_ready = sem("row_std_ready")
        unsure_ready = sem("unsure_ready")
        unsure_summed = sem("unsure_summed")
        search_step = sem("search_step")
        redo_step = sem("redo_step")
        kept_first = sem("kept_first")
        kept_split = sem("kept_split")
        kept = sem("kept")
        row_means = sem("row_means")
        deg_summed = sem("deg_summed")
        deg_taken = sem("deg_taken")
        deg_root_ready = sem("deg_root_ready")
        dinv_ready = sem("dinv_ready")
        dinv_row_ready = sem("dinv_row_ready")
        an_wide = sem("an_wide")
        an_hi_ready = sem("an_hi_ready")
        an_ready = sem("an_ready")
        scale_ready = sem("scale_ready")
        xw_ready = sem("xw_ready")
        early_wide = sem("early_wide")
        xw_wide = sem("xw_wide")
        xw_hi = sem("xw_hi")
        xw_lo = sem("xw_lo")
        x_again = [sem(f"x_again{i}") for i in range(NS)]
        mixed = sem("mixed")
        scaled = sem("scaled")
        added = sem("added")
        x_biased = sem("x_biased")
        last_added = sem("last_added")
        stored = [sem(f"stored{i}") for i in range(NS)]

        def upper_half(t, k):
            return t[:, k].bitcast(bf16).rearrange("p (n h) -> p n h", h=2)[:, :, 1]

        block = ctx.enter_context(nc.Block())

        @block.sync
        def _(sp):
            def load(g, slot):
                sp.dma_start(x_ring[:, slot], x_v[g]).then_inc(x_loaded[slot], 16)

            for j in range(G):
                sp.dma_start(x_ring[:, 0, j], x[j]).then_inc(x_first[j], 16)
            for slot in range(1, NS):
                load(slot, slot)
            sp.dma_start(w[:], adj).then_inc(s_w_in, 16)
            sp.dma_start(bias_t[:], bias.rearrange("(l a) -> l a", a=1)).then_inc(s_w_in, 16)
            with sp.Fori(1, NG // NS) as p:
                for slot in range(NS):
                    g = p * NS + slot
                    sp.wait_ge(h_ready, (g - NS + 1) * G)
                    load(g, slot)

            def load_again(g, slot):
                sp.dma_start(x_ring[:, slot], x_v[g]).then_inc(x_again[slot], 16)

            sp.wait_ge(h_ready, B)
            for slot in range(NS):
                load_again(slot, slot)

            def store(g, slot):
                sp.wait_ge(added, (g + 1) * G)
                sp.dma_start(out_v[g], h_ring[:, slot]).then_inc(stored[slot], 16)

            with sp.Fori(0, NG // NS - 1) as p:
                for slot in range(NS):
                    store(p * NS + slot, slot)
                    load_again(p * NS + slot + NS, slot)
            for slot in range(NS - 1):
                store(NG - NS + slot, slot)
            for j in range(G):
                sp.wait_ge(last_added, j + 1)
                sp.dma_start(out[B - G + j], h_ring[:, NS - 1, j]).then_inc(stored[NS - 1], 16)
            for slot in range(NS - 1):
                sp.wait_ge(stored[slot], 16 * (NG // NS))
            sp.wait_ge(stored[NS - 1], 16 * (NG // NS - 1 + G))

        @block.gpsimd
        def _(pool):
            nc.gpsimd.memset(ident[:], 0.0).then_inc(s_const, 1)
            pool.wait_ge(s_const, 1)
            nc.gpsimd.affine_select(out=ident[:], in_=ident[:], compare_op=ALU.not_equal, fill=1.0, base=0,
                                    pattern=[[-1, P]], channel_multiplier=1).then_inc(s_const, 1)

            nc.gpsimd.iota(order[:], pattern=[[1, PICK]], base=1, channel_multiplier=0,
                           allow_small_or_imprecise_dtypes=True)

            def first_half(q, i):
                if 0 <= i - 1 < NG:
                    k = ((i - 1) * G) % 4
                    pool.wait_ge(square_ready, (q - 1) * G + 1)
                    if i - 1 >= 2:
                        pool.wait_ge(summed, (q - 1) * G - 3)
                    nc.gpsimd.tensor_tensor(squares_lo[:, k], squares[:, k], upper_half(squares, k),
                                            ALU.subtract).then_inc(square_split[0], 1)
                for j in range(G):
                    if 0 <= i - 4 < NG:
                        b, k = (q - 4) * G + j, ((i - 4) * G + j) % 4
                        pool.wait_ge(hi_ready, b + 1)
                        nc.gpsimd.tensor_tensor(parts[:, b, 1, :], wide[:, k], parts[:, b, 0, :],
                                                ALU.subtract).then_inc(lo_ready, 1)
                if LEAD <= i - 1 < NG + LEAD:
                    pool.wait_ge(inv_ready, q)
                    nc.gpsimd.tensor_tensor(
                        node_norm[:, bass.ds((q - 1 - LEAD) * G, G), :].rearrange("p b c -> p (b c)"),
                        power[:, (i - 1) % 4, 0:G * NC], inv[:, (i - 1) % NS, 0:G * NC],
                        ALU.mult).then_inc(norm_kept, 1)

            for q in range(1, 5):
                first_half(q, q)
            with pool.Fori(5, 33, 4) as q:
                for i in range(5, 9):
                    first_half(q + (i - 5), i)
            for q in range(33, NG + 4):
                first_half(q, q)

            pool.wait_ge(norm_kept, NG)
            nc.gpsimd.tensor_scalar_mul(node_norm[:], node_norm[:], NORM_SCALE).then_inc(norm_scaled, 1)

            pool.wait_ge(diagonal_full, 1)
            for i in range(NC):
                d = sim[:, i, i * P:(i + 1) * P]
                last = nc.gpsimd.affine_select(out=d, in_=d, compare_op=ALU.not_equal, fill=-1.0, base=0,
                                               pattern=[[-1, P]], channel_multiplier=1)
            last.then_inc(sim_ready, 1)

            def xw_lo_part(b, k):
                pool.wait_ge(xw_hi, b + 1)
                nc.gpsimd.tensor_tensor(parts[:, b, 1, :], wide[:, k], parts[:, b, 0, :],
                                        ALU.subtract).then_inc(xw_lo, 1)

            def add_x(b, i):
                u, j = (i // G) % NS, i % G
                if j == 0:
                    pool.wait_ge(x_again[u], (b - u * G) * 2 + 16)
                pool.wait_ge(scaled, b + 1)
                y = h_ring[:, u, j, :]
                nc.gpsimd.tensor_tensor(y, y, x_ring[:, u, j, :], ALU.add).then_inc(added, 1)

            for b in range(EARLY):
                if b == EARLY_KEPT:
                    for i in range(2):
                        pool.wait_ge(kept_first, i + 1)
                        nc.gpsimd.tensor_tensor(adjacency_lo[:, i], adjacency[:, i], upper_half(adjacency, i),
                                                ALU.subtract).then_inc(kept_split, 1)
                xw_lo_part(b, b % 4)
            with pool.Fori(0, 5) as p:
                for i in range(8):
                    xw_lo_part(p * 8 + i + EARLY, (i + EARLY) % 4)
                    add_x(p * 8 + i, i)
            for b in range(40, B - G):
                if b + EARLY < B:
                    xw_lo_part(b + EARLY, (b + EARLY) % 4)
                add_x(b, b)

        @block.scalar
        def _(act):
            act.wait_ge(s_memset, 1)
            nc.scalar.activation(root[:, 1, 0:1], ones[:], ACT.Sqrt)

            def first_half(q, i):
                def relu(j):
                    b, u = (q - 1) * G + j, (i - 1) % NS
                    if j == 0:
                        act.wait_ge(ln_ready, q)
                    if i - 1 >= NS:
                        act.wait_ge(wide_ready, b + 1 - NS * G)
                    nc.scalar.activation(h_ring[:, u, j], x_ring[:, u, j], ACT.Relu, bias=shift[:, u, j:j + 1],
                                         scale=inv[:, u, G * NC + j:G * NC + j + 1]).then_inc(h_ready, 1)

                def square(j):
                    b, u = (q - 1) * G + j, (i - 1) % NS
                    act.wait_ge(h_ready, b + 1)
                    if i - 1 >= 2:
                        act.wait_ge(summed, b - 3)
                    nc.scalar.activation(squares[:, (u * G + j) % 4], h_ring[:, u, j],
                                         ACT.Square).then_inc(square_ready, 1)

                def hi_part(j):
                    b = (q - 4) * G + j
                    act.wait_ge(wide_ready, b + 1)
                    nc.scalar.activation(parts[:, b, 0, :], wide[:, ((i - 4) * G + j) % 4],
                                         ACT.Copy).then_inc(hi_ready, 1)

                new, old = 0 <= i - 1 < NG, 0 <= i - 4 < NG
                if new:
                    relu(0)
                if i < NG + LEAD:
                    act.wait_ge(power_ready, q + 1)
                    nc.scalar.activation(root[:, i % 2], power[:, i % 4], ACT.Sqrt).then_inc(root_ready, 1)
                if new:
                    square(0)
                    relu(1)
                if old:
                    hi_part(0)
                if new:
                    square(1)
                if old:
                    hi_part(1)

            for q in range(5):
                first_half(q, q)
            with act.Fori(5, 33, 4) as q:
                for i in range(5, 9):
                    first_half(q + (i - 5), i)
            for q in range(33, NG + 4):
                first_half(q, q)

            act.wait_ge(gram_done, 1)
            nc.scalar.activation(squares[:, 3], cross[:], ACT.Copy,
                                 scale=SIM_SCALE).then_inc(act_evac, 1)
            nc.scalar.activation(sim[:, 0, P:N], gram[0][:, P:N], ACT.Copy, scale=SIM_SCALE).then_inc(act_evac, 1)

            act.wait_ge(norm_scaled, 1)
            def early_scale(b):
                act.wait_ge(xw_ready, b + 1)
                if b >= 4:
                    act.wait_ge(xw_lo, b - 3)
                for c in range(NC):
                    last = nc.scalar.activation(wide[:, b % 4, c * P:(c + 1) * P], bank[b % 2][:, c * P:(c + 1) * P],
                                                ACT.Copy, scale=node_norm[:, b, c:c + 1])
                last.then_inc(early_wide, 1)

            def xw_hi_part(b, k, early=False):
                if early:
                    act.wait_ge(early_wide, b + 1)
                else:
                    act.wait_ge(xw_wide, b + 1 - EARLY)
                nc.scalar.activation(parts[:, b, 0, :], wide[:, k], ACT.Copy).then_inc(xw_hi, 1)

            early_scale(0)
            act.wait_ge(turned, 2)
            nc.scalar.activation(sim[:, 1, 0:P], gram[1][:, 0:P], ACT.Copy)
            nc.scalar.activation(sim[:, 2, 0:2 * P], gram[1][:, P:3 * P], ACT.Copy).then_inc(lower_full, 1)
            nc.scalar.activation(sim[:, 3, 0:3 * P], cross[:, 0:3 * P], ACT.Copy).then_inc(lower_full, 1)
            for b in range(1, EARLY):
                if b == EARLY_STD:
                    act.wait_ge(row_means, 1)
                    nc.scalar.activation(row_std[:], row_mean[:, :, 1], ACT.Sqrt).then_inc(row_std_ready, 1)
                if b == EARLY_DEG:
                    act.wait_ge(deg_taken, 1)
                    nc.scalar.activation(deg_root[:], deg[:], ACT.Sqrt).then_inc(deg_root_ready, 1)
                if b == EARLY_AN:
                    for c in range(NC):
                        act.wait_ge(an_wide, c + 1)
                        nc.scalar.activation(an_hi[:, c], sim[:, c], ACT.Copy).then_inc(an_hi_ready, 1)
                early_scale(b)
                xw_hi_part(b - 1, (b - 1) % 4, early=True)
            xw_hi_part(EARLY - 1, (EARLY - 1) % 4, early=True)

            def scale_and_bias(b, i):
                u, j = (i // G) % NS, i % G
                if i >= NS * G and j == 0:
                    act.wait_ge(stored[u], (b - u * G) * 2)
                act.wait_ge(mixed, b + 1)
                nc.scalar.activation(h_ring[:, u, j], gram[i % MIX_BANKS][:], ACT.Identity,
                                     bias=bias_t[:], scale=out_scale[:]).then_inc(scaled, 1)

            def second_half(b, i):
                if i + EARLY < B:
                    xw_hi_part(b + EARLY, (i + EARLY) % 4)
                scale_and_bias(b, i)

            act.wait_ge(scale_ready, 1)
            for b in range(8):
                second_half(b, b)
            with act.Fori(1, 5) as p:
                for i in range(8, 16):
                    second_half(p * 8 + (i - 8), i)
            for b in range(40, B - G):
                second_half(b, b)

        @block.vector
        def _(dve):
            def rsqrt_newton(v, approx_root, t, result, sems, count):
                def first():
                    nc.vector.reciprocal(t[:, 0], approx_root).then_inc(sems[0], 1)

                def second():
                    dve.wait_ge(sems[0], count)
                    nc.vector.scalar_tensor_tensor(out=t[:, 1], in0=v, scalar=-0.5, in1=t[:, 0],
                                                   op0=ALU.mult, op1=ALU.mult).then_inc(sems[1], 1)

                def third():
                    dve.wait_ge(sems[1], count)
                    nc.vector.tensor_tensor(t[:, 2], t[:, 1], t[:, 0], ALU.mult).then_inc(sems[2], 1)

                def fourth():
                    dve.wait_ge(sems[2], count)
                    return nc.vector.scalar_tensor_tensor(out=result, in0=t[:, 2], scalar=1.5, in1=t[:, 0],
                                                          op0=ALU.add, op1=ALU.mult)
                return first, second, third, fourth

            def bn_stats(q, i, j):
                if i == 0:
                    dve.wait_ge(x_first[j], 16)
                elif j == 0:
                    dve.wait_ge(x_loaded[i % NS], load_count(q, i))
                return nc.vector.bn_stats(stats[:, i % 2, j], x_ring[:, i % NS, j])

            def load_count(q, i):
                return (q - i % NS) * (16 // NS) + (16 if i % NS else 0)

            def first_half(q, i):
                var_cols = slice(G * NC, NQ)
                newton = rsqrt_newton(power[:, i % 4], root[:, i % 2], inv_t, inv[:, i % NS],
                                      (newton_a, newton_b, newton_c), q + 1)

                def unit_vectors(j):
                    b, u = (q - 4) * G + j, (i - 4) % NS
                    dve.wait_ge(bcast_ready, b + 1)
                    if i - 4 >= 2:
                        dve.wait_ge(lo_ready, b - 3)
                    nc.vector.scalar_tensor_tensor(out=wide[:, (u * G + j) % 4], in0=h_ring[:, u, j], scalar=XN_SCALE,
                                                   in1=bank[j][:], op0=ALU.mult, op1=ALU.mult).then_inc(wide_ready, 1)

                live = i < NG + LEAD
                if 0 <= i - 2 < NG:
                    k = ((i - 2) * G + 1) % 4
                    dve.wait_ge(square_ready, (q - 1) * G)
                    if i - 2 >= 2:
                        dve.wait_ge(summed, (q - 1) * G - 4)
                    nc.vector.tensor_tensor(squares_lo[:, k], squares[:, k], upper_half(squares, k),
                                            ALU.subtract).then_inc(square_split[1], 1)
                if i < NG:
                    dve.wait_ge(mean_ready, q + 1)
                    add_eps = nc.vector.tensor_scalar_add(power[:, i % 4, var_cols], mean_var[:, i % 4, :, 1], EPS)
                elif live:
                    add_eps = nc.vector.tensor_copy(power[:, i % 4, var_cols], power[:, (i - 1) % 4, var_cols])
                if LEAD <= i < NG + LEAD:
                    dve.wait_ge(summed, (q - LEAD + 1) * G)
                    if i >= LEAD + 4:
                        dve.wait_ge(norm_kept, q - LEAD - 3)
                    last = nc.vector.tensor_scalar_max(power[:, i % 4, 0:G * NC], small[:, 0:G * NC], 1e-24)
                    last.then_inc(power_ready, 1)
                elif live:
                    add_eps.then_inc(power_ready, 1)
                if i + 1 < NG:
                    bn_stats(q + 1, i + 1, 0)
                if live:
                    dve.wait_ge(root_ready, q + 1)
                    newton[0]()
                if i + 1 < NG:
                    bn_stats(q + 1, i + 1, 1).then_inc(stats_ready, 1)
                if live:
                    newton[1]()
                if i >= LEAD + 1:
                    unit_vectors(0)
                if live:
                    newton[2]()
                if i >= LEAD + 1:
                    unit_vectors(1)
                if live:
                    newton[3]().then_inc(inv_ready, 1)
                if i + 1 < NG:
                    dve.wait_ge(stats_ready, q + 2)
                if live:
                    dve.wait_ge(inv_ready, q + 1)
                if i < NG:
                    nc.vector.scalar_tensor_tensor(out=shift[:, i % NS], in0=mean_var[:, i % 4, :, 0], scalar=-1.0,
                                                   in1=inv[:, i % NS, var_cols], op0=ALU.mult,
                                                   op1=ALU.mult).then_inc(ln_ready, 1)
                if i + 1 < NG:
                    for j in range(G):
                        last = nc.vector.bn_aggr(mean_var[:, (i + 1) % 4, j], stats[:, (i + 1) % 2, j])
                    last.then_inc(mean_ready, 1)

            for t, v in ((ones, 1.0), (ones_hi, 1.0), (ones_lo, 1.0), (power, 1.0), (zeros, 0.0)):
                last = nc.vector.memset(t[:], v)
            last.then_inc(s_memset, 1)

            for j in range(G):
                last = bn_stats(0, 0, j)
            last.then_inc(stats_ready, 1)
            dve.wait_ge(stats_ready, 1)
            for j in range(G):
                last = nc.vector.bn_aggr(mean_var[:, 0, j], stats[:, 0, j])
            last.then_inc(mean_ready, 1)
            for q in range(6):
                first_half(q, q)
            with dve.Fori(6, 30, 4) as q:
                for i in range(6, 10):
                    first_half(q + (i - 6), i)
            for q in range(30, NG + 4):
                first_half(q, q)

            dve.wait_ge(s_w_in, 32)
            nc.vector.tensor_reduce(w_t[:, 0:1], w[:], axis=AX_X, op=ALU.max,
                                    apply_absolute_value=True).then_inc(w_max_ready, 1)
            dve.wait_ge(w_row_ready, 1)
            nc.vector.reduce_max(w_t[:, 1:2], bank[1][:, 0:P], AX_X).then_inc(dve_step, 1)
            dve.wait_ge(dve_step, 1)
            nc.vector.tensor_scalar_max(w_t[:, 2:3], w_t[:, 1:2], 2.0 ** -100).then_inc(dve_step, 1)
            dve.wait_ge(dve_step, 2)
            nc.vector.tensor_single_scalar(w_top[:].bitcast(i32), w_t[:, 2:3].bitcast(i32), 0x7F800000,
                                           ALU.bitwise_and).then_inc(dve_step, 1)
            dve.wait_ge(dve_step, 3)
            nc.vector.reciprocal(w_t[:, 3:4], w_top[:]).then_inc(dve_step, 1)
            dve.wait_ge(dve_step, 4)
            nc.vector.tensor_scalar(w[:], w[:], w_t[:, 3:4], W_SCALE, ALU.mult, ALU.mult).then_inc(dve_step, 1)
            dve.wait_ge(dve_step, 5)
            nc.vector.tensor_copy(w_hi[:], w[:]).then_inc(dve_step, 1)
            dve.wait_ge(dve_step, 6)
            nc.vector.tensor_tensor(w_lo[:], w[:], w_hi[:], ALU.subtract).then_inc(w_split_ready, 1)
            at = 6

            def step(ins):
                nonlocal at
                at += 1
                ins.then_inc(dve_step, 1)
                dve.wait_ge(dve_step, at)

            dve.wait_ge(gram_done, 1)
            for i in range(1, NC - 1):
                last = nc.vector.tensor_scalar_mul(sim[:, i, (i + 1) * P:N], gram[i][:, (i + 1) * P:N], SIM_SCALE)
            last.then_inc(dve_evac, 1)
            dve.wait_ge(act_evac, 1)
            for i in (1, 2, 3, 0):
                if i == 0:
                    dve.wait_ge(act_evac, 2)
                last = nc.vector.scalar_tensor_tensor(
                    out=sim[:, i, i * P:(i + 1) * P], in0=gram[i][:, i * P:(i + 1) * P], scalar=SIM_SCALE,
                    in1=diag_half[:, i], op0=ALU.mult, op1=ALU.add).then_inc(diagonal_read, 1)
            dve.wait_ge(diagonal_read, NC)
            sample = ((P, N), (2 * P, N), (0, 2 * P), (0, 3 * P))

            def sample_stats(i):
                return nc.vector.bn_stats(row_stats[:, i], sim[:, i, sample[i][0]:sample[i][1]])

            sample_stats(0)
            dve.wait_ge(turned, 1)
            for i in range(NC):
                d = sim[:, i, i * P:(i + 1) * P]
                last = nc.vector.tensor_tensor(d, d, small[:, i * P:(i + 1) * P], ALU.add)
            last.then_inc(diagonal_full, 1)
            dve.wait_ge(dve_evac, 1)
            sample_stats(1)
            dve.wait_ge(lower_full, 1)
            sample_stats(2)
            dve.wait_ge(lower_full, 2)
            step(sample_stats(3))
            for i in range(NC):
                last = nc.vector.bn_aggr(row_mean[:, i], row_stats[:, i])
            last.then_inc(row_means, 1)
            dve.wait_ge(row_std_ready, 1)
            dve.wait_ge(sim_ready, 1)
            nc.vector.tensor_scalar_mul(per_count[:], row_std[:], 1.0 / DENSITY)
            step(nc.vector.scalar_tensor_tensor(out=theta[:], in0=row_std[:], scalar=QUANTILE, in1=row_mean[:, :, 0],
                                                op0=ALU.mult, op1=ALU.add))

            def count_reaching(to, thresholds):
                for i in range(NC):
                    last = nc.vector.tensor_scalar(an_hi[:, i], sim[:, i], thresholds[:, i:i + 1], None,
                                                   ALU.is_ge, ALU.add, accum_out=to[:, i:i + 1])
                return last

            for gain in GAINS:
                step(count_reaching(count, theta))
                step(nc.vector.scalar_tensor_tensor(out=move[:], in0=count[:], scalar=-float(GOAL), in1=per_count[:],
                                                    op0=ALU.add, op1=ALU.mult))
                step(nc.vector.scalar_tensor_tensor(out=theta[:], in0=move[:], scalar=gain, in1=theta[:],
                                                    op0=ALU.mult, op1=ALU.add))
            count_reaching(count, theta)
            for i in range(NC):
                last = nc.vector.scalar_tensor_tensor(out=under[:, i], in0=sim[:, i], scalar=theta[:, i:i + 1],
                                                      in1=sim[:, i], op0=ALU.is_lt, op1=ALU.mult)
            step(last)
            for i in range(NC):
                for k in range(SEGS):
                    last = nc.vector.max(piece_largest[:, i, k], under[:, i, k * (N // SEGS):(k + 1) * (N // SEGS)])
            step(last)
            pieces = piece_largest[:].rearrange("p c k e -> p c (k e)")
            nc.vector.tensor_reduce(piece_least[:], piece_largest[:, :, :, 7], axis=AX_X, op=ALU.max)
            for i in range(NC):
                last = nc.vector.max(largest[:, i, 0:8], pieces[:, i])
            step(last)
            for i in range(NC):
                last = nc.vector.match_replace(pieces[:, i], largest[:, i, 0:8], pieces[:, i], -2.0)
            step(last)
            nc.vector.tensor_scalar(rank_wanted[:], count[:], -1.0, float(TOP), ALU.mult, ALU.add)
            for i in range(NC):
                last = nc.vector.max(largest[:, i, 8:16], pieces[:, i])
            step(last)
            step(nc.vector.tensor_tensor(one_hot[:], order[:, 0:PICK - 1].unsqueeze(1).to_broadcast([P, NC, PICK - 1]),
                                         rank_wanted[:].unsqueeze(2).to_broadcast([P, NC, PICK - 1]), ALU.is_equal))
            nc.vector.tensor_tensor(picked[:, 0], one_hot[:], largest[:, :, 0:PICK - 1], ALU.mult)
            step(nc.vector.tensor_tensor(picked[:, 1], one_hot[:], largest[:, :, 1:PICK], ALU.mult))
            step(nc.vector.reduce_sum(value[:].rearrange("p a c -> p (a c)"),
                                      picked[:].rearrange("p a c k -> p (a c) k"), AX_X))
            def keep(i):
                nc.vector.scalar_tensor_tensor(out=adjacency[:, i], in0=sim[:, i], scalar=value[:, 0, i:i + 1],
                                               in1=sim[:, i], op0=ALU.is_ge, op1=ALU.mult).then_inc(kept_first, 1)

            nc.vector.tensor_tensor(missed[:], piece_least[:], value[:, 1], ALU.max).then_inc(dve_step, 1)
            keep(0)
            dve.wait_ge(dve_step, at + 1)
            nc.vector.tensor_tensor(unsure[:, 0], missed[:], value[:, 0], ALU.is_ge)
            nc.vector.tensor_tensor(unsure[:, 1], piece_least[:], value[:, 0], ALU.is_ge).then_inc(dve_step, 1)
            keep(1)
            dve.wait_ge(dve_step, at + 2)
            nc.vector.reduce_max(unsure_any[:], unsure[:], AX_X).then_inc(unsure_ready, 1)
            at += 2
            for i in range(2, NC):
                keep(i)

            def split_kept(i):
                return nc.vector.tensor_tensor(adjacency_lo[:, i], adjacency[:, i], upper_half(adjacency, i),
                                               ALU.subtract)

            dve.wait_ge(unsure_summed, 1)
            step(nc.vector.tensor_copy(unsure_rows[:], small[0:1, 0:2]))
            for i in (2, 3):
                dve.wait_ge(kept_first, i + 1)
                last = split_kept(i)
            last.then_inc(dve_step, 1)
            at += 1
            again = dve.value_load(unsure_rows[0:1, 0:1], min_val=0, max_val=P)
            dve.wait_ge(dve_step, at)
            dve.wait_ge(kept_split, 2)

            redo = [0]

            def redo_wait(ins):
                redo[0] += 1
                ins.then_inc(redo_step, 1)
                dve.wait_ge(redo_step, redo[0])

            with dve.If(again > 0):
                redo_wait(nc.vector.tensor_copy(best[:].bitcast(f32), value[:, 0]))
                search = dve.value_load(unsure_rows[0:1, 1:2], min_val=0, max_val=P)
                with dve.If(search > 0):
                    nc.vector.memset(best[:], 0)
                    nc.vector.memset(bit[:], 1 << TOP_BIT).then_inc(search_step, 1)
                    dve.wait_ge(search_step, 1)
                    SEARCH = 5
                    with dve.Fori(0, TOP_BIT + 1) as it:
                        start = it * SEARCH + 1
                        nc.vector.tensor_tensor(cand[:], best[:], bit[:], ALU.bitwise_or).then_inc(search_step, 1)
                        dve.wait_ge(search_step, start + 1)
                        count_reaching(count, cand[:].bitcast(f32)).then_inc(search_step, 1)
                        dve.wait_ge(search_step, start + 2)
                        nc.vector.scalar_tensor_tensor(out=keep_bit[:], in0=count[:], scalar=float(TOP), in1=bit[:],
                                                       op0=ALU.is_ge, op1=ALU.mult).then_inc(search_step, 1)
                        dve.wait_ge(search_step, start + 3)
                        nc.vector.tensor_tensor(best[:], best[:], keep_bit[:], ALU.bitwise_or).then_inc(search_step, 1)
                        nc.vector.tensor_single_scalar(bit[:], bit[:], 1,
                                                       ALU.logical_shift_right).then_inc(search_step, 1)
                        dve.wait_ge(search_step, start + 5)
                for i in range(NC):
                    best_f = best[:, i:i + 1].bitcast(f32)
                    nc.vector.tensor_scalar(above[:, 0], sim[:, i], best_f, None, ALU.is_gt, ALU.add,
                                            accum_out=count[:, i:i + 1])
                    redo_wait(nc.vector.tensor_scalar(equal[:, 0], sim[:, i], best_f, None, ALU.is_equal))
                    nc.vector.tensor_scalar(need[:, i:i + 1], count[:, i:i + 1], -1.0, float(TOP), ALU.mult, ALU.add)
                    redo_wait(nc.vector.tensor_tensor_scan(rank[:, 0], equal[:, 0], zeros[:], 0.0, ALU.add, ALU.add))
                    redo_wait(nc.vector.scalar_tensor_tensor(out=equal[:, 0], in0=rank[:, 0], scalar=need[:, i:i + 1],
                                                             in1=equal[:, 0], op0=ALU.is_le, op1=ALU.mult))
                    redo_wait(nc.vector.tensor_tensor(above[:, 0], above[:, 0], equal[:, 0], ALU.add))
                    redo_wait(nc.vector.tensor_tensor(adjacency[:, i], sim[:, i], above[:, 0], ALU.mult))
                    redo_wait(split_kept(i))
            nc.vector.engine_nop().then_inc(kept, 1)

            dve.wait_ge(deg_summed, 1)
            nc.vector.tensor_scalar_max(deg[:], small[:, 0:NC], 2.0 ** -100).then_inc(deg_taken, 1)
            dve.wait_ge(deg_root_ready, 1)
            newton = rsqrt_newton(deg[:], deg_root[:], deg_t, deg_t[:, 3], (newton_a, newton_b, newton_c), NG + LEAD + 1)
            for part in newton[:3]:
                part()
            step(newton[3]())
            step(nc.vector.scalar_tensor_tensor(out=dinv[:], in0=deg[:], scalar=2.0 ** -100, in1=deg_t[:, 3],
                                                op0=ALU.is_gt, op1=ALU.mult))
            nc.vector.reduce_max(d_top[:, 0:1], dinv[:], AX_X).then_inc(dinv_ready, 1)
            dve.wait_ge(dinv_row_ready, 1)
            step(nc.vector.reduce_max(d_top[:, 1:2], cross[:, 0:P], AX_X))
            step(nc.vector.tensor_scalar_max(d_top[:, 1:2], d_top[:, 1:2], 2.0 ** -5))
            step(nc.vector.tensor_single_scalar(d_top[:, 2:3].bitcast(i32), d_top[:, 1:2].bitcast(i32), 0x7F800000,
                                                ALU.bitwise_and))
            step(nc.vector.reciprocal(d_top[:, 3:4], d_top[:, 2:3]))
            step(nc.vector.tensor_scalar(an_scale[:], d_top[:, 3:4], d_top[:, 3:4], DINV_SCALE * DINV_SCALE,
                                         ALU.mult, ALU.mult))
            step(nc.vector.tensor_scalar_mul(dinv_scaled[:], dinv[:], an_scale[:]))
            dve.wait_ge(dinv_row_ready, 2)

            def an(i):
                nc.vector.scalar_tensor_tensor(out=sim[:, i], in0=adjacency[:, i], scalar=dinv_scaled[:, i:i + 1],
                                               in1=small[:], op0=ALU.mult, op1=ALU.mult).then_inc(an_wide, 1)

            an(0)
            an(1)
            for i in range(NC):
                dve.wait_ge(an_hi_ready, i + 1)
                nc.vector.tensor_tensor(an_lo[:, i], sim[:, i], an_hi[:, i], ALU.subtract).then_inc(an_ready, 1)
                if i + 2 < NC:
                    an(i + 2)
            step(nc.vector.tensor_scalar(out_scale[:], d_top[:, 2:3], d_top[:, 2:3], w_top[:], ALU.mult, ALU.mult))
            nc.vector.tensor_scalar_mul(out_scale[:], out_scale[:],
                                        1.0 / (XW_SCALE * DINV_SCALE * DINV_SCALE)).then_inc(scale_ready, 1)

            def scale_by_norm(b, i):
                dve.wait_ge(xw_ready, b + 1)
                dve.wait_ge(xw_lo, b - 3)
                nc.vector.tensor_tensor(
                    wide[:, i % 4].rearrange("p (c l) -> p c l", c=NC), bank[i % 2][:].rearrange("p (c l) -> p c l", c=NC),
                    node_norm[:, b, :].unsqueeze(2).to_broadcast([P, NC, P]), ALU.mult).then_inc(xw_wide, 1)

            with dve.Fori(EARLY // 4, B // 4) as p:
                for i in range(4):
                    scale_by_norm(p * 4 + i, i)

            dve.wait_ge(x_again[NS - 1], 16 * (NG // NS))
            last_x = x_ring[:, NS - 1].rearrange("p g n -> p (g n)")
            nc.vector.tensor_scalar(last_x, last_x, bias_t[:], None, ALU.add).then_inc(x_biased, 1)
            dve.wait_ge(x_biased, 1)
            dve.wait_ge(stored[NS - 1], 16 * (NG // NS - 1))
            for j in range(G):
                dve.wait_ge(mixed, B - G + j + 1)
                nc.vector.scalar_tensor_tensor(out=h_ring[:, NS - 1, j], in0=gram[(B - G + j) % MIX_BANKS][:],
                                               scalar=out_scale[:], in1=x_ring[:, NS - 1, j], op0=ALU.mult,
                                               op1=ALU.add).then_inc(last_added, 1)

        @block.tensor
        def _(pe):
            pe.wait_ge(s_memset, 1)
            for t in gram + [cross]:
                nc.tensor.matmul(t[:], zeros[:, 0:P], zeros[:], start=True, stop=False, skip_group_check=True)
            pe.wait_ge(s_const, 2)

            def first_half(q, i):
                def broadcast(j):
                    b, r = (q - 4) * G + j, (i - 1) % NS
                    if j == 0:
                        pe.wait_ge(inv_ready, q)
                    if i - 4 >= 1:
                        pe.wait_ge(wide_ready, b - 1)
                    for c in range(NC):
                        k = j * NC + c
                        last = nc.tensor.matmul(bank[j][:, c * P:(c + 1) * P], inv[:, r, k:k + 1].to_broadcast([P, P]),
                                                ident[:], is_transpose=True, start=True, stop=True)
                    last.then_inc(bcast_ready, 1)

                def sum_squares(j):
                    b, k = (q - 2) * G + j, ((i - 2) * G + j) % 4
                    if j == 0 and i - 2 >= 1:
                        pe.wait_ge(power_ready, q - 2 + LEAD)
                    pe.wait_ge(square_split[j], q - 1)
                    upper = upper_half(squares, k)
                    for c in range(NC):
                        at = small[:, j * NC + c:j * NC + c + 1]
                        nodes = slice(c * P, (c + 1) * P)
                        nc.tensor.matmul(at, upper[:, nodes], ones_hi[:], start=True, stop=False)
                        last = nc.tensor.matmul(at, squares_lo[:, k, nodes], ones_lo[:], start=False, stop=True)
                    last.then_inc(summed, 1)

                for j in range(G):
                    if 0 <= i - 4 < NG:
                        broadcast(j)
                for j in range(G):
                    if 0 <= i - 2 < NG:
                        sum_squares(j)
                    if 0 <= i - 5 < NG:
                        gram_step((q - 5) * G + j, i - 5 == NG - 1 and j == G - 1)

            def gram_step(b, final):
                pe.wait_ge(lo_ready, b + 1)
                for i in range(NC):
                    own = slice(i * P, (i + 1) * P)
                    hi_i, lo_i = parts[:, b, 0, own], parts[:, b, 1, own]
                    nc.tensor.matmul(gram[i][:, i * P:N], hi_i, parts[:, b, 0, i * P:N],
                                     start=False, stop=final and i == NC - 1, skip_group_check=True)
                    last = nc.tensor.matmul(cross[:, own], hi_i, lo_i, start=False, stop=final, skip_group_check=True)
                    if i < NC - 1:
                        right = slice((i + 1) * P, N)
                        nc.tensor.matmul(gram[i][:, right], hi_i, parts[:, b, 1, right],
                                         start=False, stop=False, skip_group_check=True)
                        nc.tensor.matmul(gram[i][:, right], lo_i, parts[:, b, 0, right],
                                         start=False, stop=final, skip_group_check=True)
                if final:
                    last.then_inc(gram_done, 1)

            for q in range(2, 5):
                first_half(q, q)
            with pe.Fori(5, 33, 4) as q:
                for i in range(5, 9):
                    first_half(q + (i - 5), i)
            for q in range(33, NG + 4):
                first_half(q, q)
            pe.wait_ge(wide_ready, B)
            pe.wait_ge(w_max_ready, 1)
            nc.tensor.matmul(bank[1][:, 0:P], w_t[:, 0:1].to_broadcast([P, P]), ident[:], is_transpose=True,
                             start=True, stop=True).then_inc(w_row_ready, 1)
            first_half(NG + 4, NG + 4)

            pe.wait_ge(w_split_ready, 1)

            def project(b, i):
                if 2 <= i < EARLY + 2:
                    pe.wait_ge(early_wide, b - 1)
                elif i >= 2:
                    pe.wait_ge(xw_wide, b - 1 - EARLY)
                for c in range(NC):
                    to = bank[i % 2][:, c * P:(c + 1) * P]
                    nodes = slice(c * P, (c + 1) * P)
                    nc.tensor.matmul(to, parts[:, b, 0, nodes], w_hi[:], start=True, stop=False)
                    nc.tensor.matmul(to, parts[:, b, 0, nodes], w_lo[:], start=False, stop=False)
                    last = nc.tensor.matmul(to, parts[:, b, 1, nodes], w_hi[:], start=False, stop=True)
                last.then_inc(xw_ready, 1)

            project(0, 0)

            pe.wait_ge(act_evac, 1)
            for i in range(NC):
                last = nc.tensor.transpose(small[:, i * P:(i + 1) * P], diag_half[:, i], ident[:])
            last.then_inc(turned, 1)
            pe.wait_ge(act_evac, 2)
            pe.wait_ge(dve_evac, 1)
            for k, (i, j) in enumerate(((0, 3), (1, 3), (2, 3))):
                nc.tensor.transpose(cross[:, k * P:(k + 1) * P], sim[:, i, j * P:(j + 1) * P], ident[:])
            pe.wait_ge(diagonal_read, 1)
            for k, (i, j) in enumerate(((0, 1), (0, 2), (1, 2))):
                last = nc.tensor.transpose(gram[1][:, k * P:(k + 1) * P], sim[:, i, j * P:(j + 1) * P], ident[:])
            last.then_inc(turned, 1)

            for b in range(1, EARLY_FLAG):
                project(b, b)

            pe.wait_ge(unsure_ready, 1)
            nc.tensor.matmul(small[0:1, 0:2], ones[:], unsure_any[:], start=True,
                             stop=True).then_inc(unsure_summed, 1)

            for b in range(EARLY_FLAG, EARLY_DEG):
                project(b, b)
            pe.wait_ge(kept, 1)
            for d in range(NC):
                for c in range(NC):
                    nodes = slice(d * P, (d + 1) * P)
                    nc.tensor.matmul(small[:, d:d + 1], upper_half(adjacency, c)[:, nodes], ones_hi[:],
                                     start=c == 0, stop=False)
                    last = nc.tensor.matmul(small[:, d:d + 1], adjacency_lo[:, c, nodes], ones_lo[:],
                                            start=False, stop=c == NC - 1)
            last.then_inc(deg_summed, 1)
            for b in range(EARLY_DEG, EARLY_ROW):
                project(b, b)
            pe.wait_ge(dinv_ready, 1)
            nc.tensor.matmul(cross[:, 0:P], d_top[:, 0:1].to_broadcast([P, P]), ident[:], is_transpose=True,
                             start=True, stop=True).then_inc(dinv_row_ready, 1)
            for c in range(NC):
                last = nc.tensor.matmul(small[:, c * P:(c + 1) * P], dinv[:, c:c + 1].to_broadcast([P, P]), ident[:],
                                        is_transpose=True, start=True, stop=True)
            last.then_inc(dinv_row_ready, 1)
            for b in range(EARLY_ROW, MADE[0]):
                project(b, b)

            def mix(b, i):
                to = gram[i % MIX_BANKS]
                pe.wait_ge(scaled, b + 1 - MIX_BANKS)
                pe.wait_ge(xw_lo, b + 1)
                for c in range(NC):
                    cols = slice(c * P, (c + 1) * P)
                    nc.tensor.matmul(to[:], parts[:, b, 0, cols], an_hi[:, c], start=c == 0, stop=False)
                    nc.tensor.matmul(to[:], parts[:, b, 1, cols], an_hi[:, c], start=False, stop=False)
                    last = nc.tensor.matmul(to[:], parts[:, b, 0, cols], an_lo[:, c], start=False, stop=c == NC - 1)
                last.then_inc(mixed, 1)

            pe.wait_ge(lower_full, 2)
            pe.wait_ge(xw_lo, MIX_BANKS)
            for c in range(NC):
                cols = slice(c * P, (c + 1) * P)
                pe.wait_ge(an_hi_ready, c + 1)
                for b in range(MIX_BANKS):
                    nc.tensor.matmul(gram[b][:], parts[:, b, 0, cols], an_hi[:, c], start=c == 0, stop=False)
                    nc.tensor.matmul(gram[b][:], parts[:, b, 1, cols], an_hi[:, c], start=False, stop=False)
                pe.wait_ge(an_ready, c + 1)
                for b in range(MIX_BANKS):
                    last = nc.tensor.matmul(gram[b][:], parts[:, b, 0, cols], an_lo[:, c], start=False,
                                            stop=c == NC - 1)
                    if c == NC - 1:
                        last.then_inc(mixed, 1)
                for b in range(MADE[c], MADE[c + 1]):
                    project(b, b)
            def second_half(b, i):
                mix(b, i)
                if i + EARLY < B:
                    project(b + EARLY, i + EARLY)

            with pe.Fori(1, (B - EARLY) // 4) as p:
                for i in range(4, 8):
                    second_half(p * 4 + (i - 4), i)
            with pe.Fori((B - EARLY) // 4, B // 4) as p:
                for i in range(B - EARLY, B - EARLY + 4):
                    mix(p * 4 + (i - (B - EARLY)), i)


_INS = ['x', 'adj', 'L0_gnn_bias']
_OUTS = [((64, 128, 512), 'float32')]


def kernel(**inputs):
    import numpy as _np
    import concourse.bacc as _bacc
    from concourse import mybir as _mybir
    from concourse.bass_utils import run_bass_kernel_spmd as _run

    nc = _bacc.Bacc("TRN2", target_bir_lowering=False, num_devices=1)
    arrays, args = {}, []
    for name in _INS:
        a = _np.ascontiguousarray(inputs[name])
        arrays[f"in_{name}_dram"] = a
        args.append(nc.dram_tensor(f"in_{name}_dram", a.shape, _mybir.dt.from_np(a.dtype), kind="ExternalInput").ap())
    for i, (shape, dtype) in enumerate(_OUTS):
        dt = _mybir.dt.from_np(_np.dtype(dtype))
        args.append(nc.dram_tensor(f"out_{i}_dram", shape, dt, kind="ExternalOutput").ap())
    adaptive_gcn_block(nc, *args)
    r = _run(nc, [arrays], core_ids=[0])
    return r.results[0]["out_0_dram"]
```
